# Optimizing a Trainium2 kernel written in Bass

```python
import numpy as np
import jax
import jax.numpy as jnp

def _softmax(x, axis=-1):
    return jax.nn.softmax(x, axis=axis)

def _gelu(x):
    return jax.nn.gelu(x, approximate=True)

def _silu(x):
    return jax.nn.silu(x)

def _sigmoid(x):
    return jax.nn.sigmoid(x)

def _layernorm(x, axis=-1, eps=1e-05):
    m = jnp.mean(x, axis=axis, keepdims=True)
    v = jnp.var(x, axis=axis, keepdims=True)
    return (x - m) / jnp.sqrt(v + eps)

def _scatter_add(tgt, idx, src, axis=0):
    return tgt.at[idx].add(src)

def _segment_sum(src, seg, n):
    return jax.ops.segment_sum(src, seg, n)
kernel_name = 'mk_dlrm_tower_d1_rec_r8_9862b5'

def setup_inputs(seed: int=0):
    np.random.seed(seed)
    _w = jnp.asarray

    def _rec_inputs():
        import jax
        import jax.numpy as jnp
        _tk = jax.random.key(seed)
        dense_ctx = jax.random.normal(jax.random.fold_in(_tk, 190), (2048, 16), jnp.float32)
        ids = jnp.stack([jax.random.randint(jax.random.fold_in(_tk, 200 + f), (2048,), 0, v, jnp.int32) for f, v in enumerate([125000, 12500, 12500, 1250, 1000, 1000, 12500, 1000, 12500, 12500, 1250, 1000, 1250, 1000, 1250, 12500, 1000, 12500, 1000, 1250, 1250, 1000, 1000, 1000, 1250, 1000, 1000])], axis=1)
        tbl_0 = 0.05 * jax.random.normal(jax.random.fold_in(_tk, 500 + 0), (125000, 128), jnp.float32)
        tbl_1 = 0.05 * jax.random.normal(jax.random.fold_in(_tk, 500 + 1), (12500, 128), jnp.float32)
        tbl_2 = 0.05 * jax.random.normal(jax.random.fold_in(_tk, 500 + 2), (12500, 128), jnp.float32)
        tbl_3 = 0.05 * jax.random.normal(jax.random.fold_in(_tk, 500 + 3), (1250, 128), jnp.float32)
        tbl_4 = 0.05 * jax.random.normal(jax.random.fold_in(_tk, 500 + 4), (1000, 128), jnp.float32)
        tbl_5 = 0.05 * jax.random.normal(jax.random.fold_in(_tk, 500 + 5), (1000, 128), jnp.float32)
        tbl_6 = 0.05 * jax.random.normal(jax.random.fold_in(_tk, 500 + 6), (12500, 128), jnp.float32)
        tbl_7 = 0.05 * jax.random.normal(jax.random.fold_in(_tk, 500 + 7), (1000, 128), jnp.float32)
        tbl_8 = 0.05 * jax.random.normal(jax.random.fold_in(_tk, 500 + 8), (12500, 128), jnp.float32)
        tbl_9 = 0.05 * jax.random.normal(jax.random.fold_in(_tk, 500 + 9), (12500, 128), jnp.float32)
        tbl_10 = 0.05 * jax.random.normal(jax.random.fold_in(_tk, 500 + 10), (1250, 128), jnp.float32)
        tbl_11 = 0.05 * jax.random.normal(jax.random.fold_in(_tk, 500 + 11), (1000, 128), jnp.float32)
        tbl_12 = 0.05 * jax.random.normal(jax.random.fold_in(_tk, 500 + 12), (1250, 128), jnp.float32)
        tbl_13 = 0.05 * jax.random.normal(jax.random.fold_in(_tk, 500 + 13), (1000, 128), jnp.float32)
        tbl_14 = 0.05 * jax.random.normal(jax.random.fold_in(_tk, 500 + 14), (1250, 128), jnp.float32)
        tbl_15 = 0.05 * jax.random.normal(jax.random.fold_in(_tk, 500 + 15), (12500, 128), jnp.float32)
        tbl_16 = 0.05 * jax.random.normal(jax.random.fold_in(_tk, 500 + 16), (1000, 128), jnp.float32)
        tbl_17 = 0.05 * jax.random.normal(jax.random.fold_in(_tk, 500 + 17), (12500, 128), jnp.float32)
        tbl_18 = 0.05 * jax.random.normal(jax.random.fold_in(_tk, 500 + 18), (1000, 128), jnp.float32)
        tbl_19 = 0.05 * jax.random.normal(jax.random.fold_in(_tk, 500 + 19), (1250, 128), jnp.float32)
        tbl_20 = 0.05 * jax.random.normal(jax.random.fold_in(_tk, 500 + 20), (1250, 128), jnp.float32)
        tbl_21 = 0.05 * jax.random.normal(jax.random.fold_in(_tk, 500 + 21), (1000, 128), jnp.float32)
        tbl_22 = 0.05 * jax.random.normal(jax.random.fold_in(_tk, 500 + 22), (1000, 128), jnp.float32)
        tbl_23 = 0.05 * jax.random.normal(jax.random.fold_in(_tk, 500 + 23), (1000, 128), jnp.float32)
        tbl_24 = 0.05 * jax.random.normal(jax.random.fold_in(_tk, 500 + 24), (1250, 128), jnp.float32)
        tbl_25 = 0.05 * jax.random.normal(jax.random.fold_in(_tk, 500 + 25), (1000, 128), jnp.float32)
        tbl_26 = 0.05 * jax.random.normal(jax.random.fold_in(_tk, 500 + 26), (1000, 128), jnp.float32)
        _rk = jax.random.fold_in(_tk, 7)
        W_top1 = 0.0521996 * jax.random.normal(jax.random.fold_in(_tk, 801), (367, 512), jnp.float32)
        W_top2 = 0.0441942 * jax.random.normal(jax.random.fold_in(_tk, 802), (512, 256), jnp.float32)
        W_top3 = 0.0625 * jax.random.normal(jax.random.fold_in(_tk, 803), (256, 1), jnp.float32)
        b_top1 = jnp.zeros((512,), jnp.float32)
        b_top2 = jnp.zeros((256,), jnp.float32)
        return (dense_ctx, ids, tbl_0, tbl_1, tbl_2, tbl_3, tbl_4, tbl_5, tbl_6, tbl_7, tbl_8, tbl_9, tbl_10, tbl_11, tbl_12, tbl_13, tbl_14, tbl_15, tbl_16, tbl_17, tbl_18, tbl_19, tbl_20, tbl_21, tbl_22, tbl_23, tbl_24, tbl_25, tbl_26, W_top1, b_top1, W_top2, b_top2, W_top3)
    dense_ctx, ids, tbl_0, tbl_1, tbl_2, tbl_3, tbl_4, tbl_5, tbl_6, tbl_7, tbl_8, tbl_9, tbl_10, tbl_11, tbl_12, tbl_13, tbl_14, tbl_15, tbl_16, tbl_17, tbl_18, tbl_19, tbl_20, tbl_21, tbl_22, tbl_23, tbl_24, tbl_25, tbl_26, W_top1, b_top1, W_top2, b_top2, W_top3 = _rec_inputs()

    def _L0_rec_setup():
        import jax, jax.numpy as jnp
        import numpy as np
        key = jax.random.key(seed)
        B, F, D = (2048, 27, 128)
        inputs = jax.random.normal(key, (B, F, D), dtype=jnp.float32)
        return {'inputs': inputs, 'num_feas': F}
    _L0_rec_all = _L0_rec_setup()
    _L0_rec_in = {k: v for k, v in _L0_rec_all.items() if k in ()}
    del _L0_rec_all
    return {'dense_ctx': dense_ctx, 'ids': ids, 'tbl_0': tbl_0, 'tbl_1': tbl_1, 'tbl_2': tbl_2, 'tbl_3': tbl_3, 'tbl_4': tbl_4, 'tbl_5': tbl_5, 'tbl_6': tbl_6, 'tbl_7': tbl_7, 'tbl_8': tbl_8, 'tbl_9': tbl_9, 'tbl_10': tbl_10, 'tbl_11': tbl_11, 'tbl_12': tbl_12, 'tbl_13': tbl_13, 'tbl_14': tbl_14, 'tbl_15': tbl_15, 'tbl_16': tbl_16, 'tbl_17': tbl_17, 'tbl_18': tbl_18, 'tbl_19': tbl_19, 'tbl_20': tbl_20, 'tbl_21': tbl_21, 'tbl_22': tbl_22, 'tbl_23': tbl_23, 'tbl_24': tbl_24, 'tbl_25': tbl_25, 'tbl_26': tbl_26, 'W_top1': W_top1, 'b_top1': b_top1, 'W_top2': W_top2, 'b_top2': b_top2, 'W_top3': W_top3}

def reference(dense_ctx, ids, tbl_0, tbl_1, tbl_2, tbl_3, tbl_4, tbl_5, tbl_6, tbl_7, tbl_8, tbl_9, tbl_10, tbl_11, tbl_12, tbl_13, tbl_14, tbl_15, tbl_16, tbl_17, tbl_18, tbl_19, tbl_20, tbl_21, tbl_22, tbl_23, tbl_24, tbl_25, tbl_26, W_top1, b_top1, W_top2, b_top2, W_top3):
    import jax
    import jax.numpy as jnp

    def _L0_rec_ref(inputs, num_feas):
        import jax, jax.numpy as jnp
        import numpy as np
        dot_products = jnp.einsum('bnd,bmd->bnm', inputs, inputs)
        r, c = np.tril_indices(num_feas, k=-1)
        flat_interactions = dot_products[:, c, r]
        return flat_interactions
    e = jnp.stack([tbl_0[ids[:, 0]], tbl_1[ids[:, 1]], tbl_2[ids[:, 2]], tbl_3[ids[:, 3]], tbl_4[ids[:, 4]], tbl_5[ids[:, 5]], tbl_6[ids[:, 6]], tbl_7[ids[:, 7]], tbl_8[ids[:, 8]], tbl_9[ids[:, 9]], tbl_10[ids[:, 10]], tbl_11[ids[:, 11]], tbl_12[ids[:, 12]], tbl_13[ids[:, 13]], tbl_14[ids[:, 14]], tbl_15[ids[:, 15]], tbl_16[ids[:, 16]], tbl_17[ids[:, 17]], tbl_18[ids[:, 18]], tbl_19[ids[:, 19]], tbl_20[ids[:, 20]], tbl_21[ids[:, 21]], tbl_22[ids[:, 22]], tbl_23[ids[:, 23]], tbl_24[ids[:, 24]], tbl_25[ids[:, 25]], tbl_26[ids[:, 26]]], axis=1)
    z = _L0_rec_ref(e, 27)
    z = z.reshape(z.shape[0], -1)
    h = jnp.concatenate([z, dense_ctx], axis=1)
    h = jnp.maximum(h @ W_top1 + b_top1, 0.0)
    h = jnp.maximum(h @ W_top2 + b_top2, 0.0)
    y = h @ W_top3
    return y

_drawn_inputs = setup_inputs


def setup_inputs(seed=0):
    import zlib

    import numpy as np

    out = dict(_drawn_inputs(seed))
    spreads = {'b_top1': (0.0, 0.1), 'b_top2': (0.0, 0.1)}
    factors = {}
    for name, (base, spread) in spreads.items():
        noise = np.random.default_rng([zlib.crc32(name.encode()), seed]).standard_normal(out[name].shape)
        drawn = base * np.exp(spread * noise) if base else spread * noise
        out[name] = jnp.asarray(drawn.astype(out[name].dtype))
    for name, factor in factors.items():
        out[name] = (out[name] * factor).astype(out[name].dtype)
    return out
```

```python
import concourse.bass as bass
from concourse import mybir
from contextlib import ExitStack

BATCH = 2048
FEATURES = 27
DIM = 128
DENSE = 16
HIDDEN1 = 512
HIDDEN2 = 256
P = 128

CHUNK = 256
N_CHUNKS = BATCH // CHUNK
GROUP = 4
LANE = CHUNK // GROUP
HALVES = CHUNK // P
COLS = GROUP * FEATURES
PAIRS = 2
PAIR_USED = GROUP // PAIRS * FEATURES
PAIR_COLS = 64

DIST = (FEATURES - 1) // 2
N_TILE = FEATURES // 3
PAIR_ROWS = N_TILE * DIST
DENSE_ROWS = (P - PAIR_ROWS, DENSE - (P - PAIR_ROWS), 0)
K_ROWS = tuple(PAIR_ROWS + d for d in DENSE_ROWS)

F_PER_SLOT = 4
SLOT_FEATURES = [list(range(f, min(f + F_PER_SLOT, FEATURES))) for f in range(0, FEATURES, F_PER_SLOT)]
SLOTS = [(h, g) for h in range(HALVES) for g in range(len(SLOT_FEATURES))]
N_FILLS = len(SLOTS)
T_PER_BANK = 4
N_GRAMS = LANE // T_PER_BANK
MIRROR = DIST
X_ROWS = FEATURES + MIRROR


def step_order(with_fill, with_mlp):
    order, fills = [], 0
    for b in range(N_GRAMS):
        order.append(("gram", b))
        if with_fill:
            while fills * N_GRAMS < N_FILLS * (b + 1):
                order.append(("fill", fills))
                fills += 1
        if with_mlp and b in (7, 10, 13):
            order.append((("layer1", "layer2", "layer3")[(b - 7) // 3], 0))
    return order


def dlrm_tower(nc, dense_t, ids, tables, w1, b1, w2, b2, w3, y_out):
    fp32, i32 = mybir.dt.float32, mybir.dt.int32
    ALU, ACT = mybir.AluOpType, mybir.ActivationFunctionType
    o1_tiles, o2_tiles = HIDDEN1 // P, HIDDEN2 // P

    with ExitStack() as ctx:
        def sbuf(name, shape, dt=fp32):
            return ctx.enter_context(nc.sbuf_tensor(name, shape, dt))

        def psum(name):
            return ctx.enter_context(nc.psum_tensor(name, [P, 512], fp32))

        def semaphore(name):
            return ctx.enter_context(nc.semaphore(name))

        x_dram = [nc.dram_tensor(f"gram_dram{p}", [X_ROWS, FEATURES, GROUP, LANE], fp32, kind="Internal").ap()
                  for p in range(2)]

        identity = sbuf("identity", [P, P])
        index = [sbuf(f"index{p}", [P, HALVES, FEATURES], i32) for p in range(2)]
        rows = [sbuf(f"rows{k}", [P, len(SLOT_FEATURES[g]) * DIM]) for k, (h, g) in enumerate(SLOTS)]
        emb = [sbuf(f"emb{p}", [P, LANE, PAIRS, PAIR_COLS]) for p in range(2)]
        gram = [sbuf(f"gram{p}", [P, 2 * FEATURES, LANE]) for p in range(2)]
        z = [sbuf(f"z{p}", [P, 3, CHUNK]) for p in range(2)]
        w1_sb = sbuf("w1_sb", [P, 3, HIDDEN1])
        w2_sb = sbuf("w2_sb", [P, o1_tiles, HIDDEN2])
        w3_sb = sbuf("w3_sb", [P, o2_tiles])
        b1_sb = sbuf("b1_sb", [P, o1_tiles])
        b2_sb = sbuf("b2_sb", [P, o2_tiles])
        h1 = sbuf("h1", [P, o1_tiles, CHUNK])
        h2 = sbuf("h2", [P, o2_tiles, CHUNK])
        y_sb = [sbuf(f"y_sb{p}", [1, CHUNK]) for p in range(2)]

        fill_ps = [psum(f"fill_ps{i}") for i in range(2)]
        gram_ps = [psum(f"gram_ps{i}") for i in range(2)]
        h1_ps = [psum(f"h1_ps{i}") for i in range(2)]
        h2_ps = psum("h2_ps")
        y_ps = psum("y_ps")

        weights_in = semaphore("weights_in")
        ident_zero = semaphore("ident_zero")
        ident_ready = semaphore("ident_ready")
        pad_ready = semaphore("pad_ready")
        index_ready = [semaphore(f"index_ready{p}") for p in range(2)]
        rows_in = [semaphore(f"rows_in{k}") for k in range(len(SLOTS))]
        fill_full = semaphore("fill_full")
        fill_out = semaphore("fill_out")
        gram_full = semaphore("gram_full")
        gram_out_act = semaphore("gram_out_act")
        gram_out_dve = semaphore("gram_out_dve")
        x_written = [semaphore(f"x_written{p}") for p in range(2)]
        z_ready = [semaphore(f"z_ready{p}") for p in range(2)]
        l1_full = semaphore("l1_full")
        h1_ready = semaphore("h1_ready")
        l2_full = semaphore("l2_full")
        h2_ready = semaphore("h2_ready")
        l3_full = semaphore("l3_full")
        y_ready = semaphore("y_ready")
        y_stored = [semaphore(f"y_stored{p}") for p in range(2)]

        sp_passed = semaphore("sp_passed")
        pool_passed = semaphore("pool_passed")

        N_WEIGHTS = 7
        X_WRITES = 2 * GROUP
        Z_READS = 3 + 2

        def gram_block(p, q, b):
            return gram[p][64 * q:64 * q + 2 * FEATURES, :, b * T_PER_BANK:(b + 1) * T_PER_BANK]

        def gram_block_ps(q, b):
            src = gram_ps[b % 2][64 * q:64 * q + 2 * FEATURES, 0:T_PER_BANK * COLS]
            return src.rearrange("m (t c) -> m c t", c=COLS)[:, q * 2 * FEATURES:(q + 1) * 2 * FEATURES, :]

        def settle(engine):
            engine.sem_inc(sp_passed if engine is nc.sync else pool_passed, 1)

        block = ctx.enter_context(nc.Block())

        @block.sync
        def _(sp):
            def load_index(c, p):
                src = ids[bass.ds(c * CHUNK, CHUNK), :].rearrange("(h p) f -> p h f", p=P)
                sp.dma_start(index[p][:, :, :], src).then_inc(index_ready[p], 16)

            load_index(0, 0)
            load_index(1, 1)
            k0 = 0
            for k in range(3):
                sp.dma_start(w1_sb[0:K_ROWS[k], k, :], w1[k0:k0 + K_ROWS[k], :]).then_inc(weights_in, 16)
                k0 += K_ROWS[k]
            sp.dma_start(w2_sb[:, :, :], w2.rearrange("(k p) o -> p k o", p=P)).then_inc(weights_in, 16)
            sp.dma_start(w3_sb[:, :], w3).then_inc(weights_in, 16)
            sp.dma_start(b1_sb[:, :], b1).then_inc(weights_in, 16)
            sp.dma_start(b2_sb[:, :], b2).then_inc(weights_in, 16)

            def step(c, p, use, reload, reuse):
                if reload:
                    sp.wait_ge(fill_full, (c + 1) * N_FILLS)
                    settle(sp)
                    load_index(c + 2, p)
                sp.wait_ge(gram_out_act, (c + 1) * N_GRAMS)
                sp.wait_ge(gram_out_dve, (c + 1) * N_GRAMS)
                if reuse:
                    sp.wait_ge(z_ready[p], use * 16 * Z_READS)
                settle(sp)
                for s in range(GROUP):
                    r = 64 * (s // 2) + FEATURES * (s % 2)
                    cols = slice(FEATURES * (s % 2), FEATURES * (s % 2 + 1))
                    sp.dma_start(x_dram[p][0:FEATURES, :, s, :], gram[p][r:r + FEATURES, cols, :]
                                 ).then_inc(x_written[p], 16)
                    sp.dma_start(x_dram[p][FEATURES:X_ROWS, :, s, :], gram[p][r:r + MIRROR, cols, :]
                                 ).then_inc(x_written[p], 16)
                sp.wait_ge(x_written[p], (use + 1) * 16 * X_WRITES)
                settle(sp)
                if reuse:
                    sp.wait_ge(l1_full, c - 1)
                settle(sp)
                row = FEATURES * CHUNK
                for k in range(3):
                    n0 = k * N_TILE
                    src = bass.AP(x_dram[p].tensor, (n0 + 1) * row + n0 * CHUNK,
                                  [[row + CHUNK, N_TILE], [row, DIST], [1, CHUNK]])
                    sp.dma_start(z[p][0:PAIR_ROWS, k, :], src).then_inc(z_ready[p], 16)
                sp.dma_start(z[p][PAIR_ROWS:K_ROWS[0], 0, :],
                             dense_t[0:DENSE_ROWS[0], bass.ds(c * CHUNK, CHUNK)]).then_inc(z_ready[p], 16)
                sp.dma_start(z[p][PAIR_ROWS:K_ROWS[1], 1, :],
                             dense_t[DENSE_ROWS[0]:DENSE, bass.ds(c * CHUNK, CHUNK)]).then_inc(z_ready[p], 16)

            def store(c, p):
                sp.wait_ge(y_ready, c + 1)
                settle(sp)
                sp.dma_start(y_out[bass.ds(c * CHUNK, CHUNK), :].rearrange("b o -> o b"),
                             y_sb[p][:, :]).then_inc(y_stored[p], 16)

            step(0, 0, 0, True, False)
            step(1, 1, 0, True, False)
            store(0, 0)
            with sp.Fori(0, N_CHUNKS // 2 - 2) as i:
                step(i * 2 + 2, 0, i + 1, True, True)
                store(i * 2 + 1, 1)
                step(i * 2 + 3, 1, i + 1, True, True)
                store(i * 2 + 2, 0)
            last = N_CHUNKS - 2
            step(last, 0, last // 2, False, True)
            store(last - 1, 1)
            step(last + 1, 1, last // 2, False, True)
            store(last, 0)
            store(last + 1, 1)
            for p in range(2):
                sp.wait_ge(y_stored[p], 16 * N_CHUNKS // 2)

        @block.gpsimd
        def _(pool):
            nc.gpsimd.memset(identity[:, :], 0.0).then_inc(ident_zero, 1)
            pool.wait_ge(ident_zero, 1)
            nc.gpsimd.affine_select(out=identity[:, :], in_=identity[:, :], compare_op=ALU.not_equal, fill=1.0,
                                    base=0, pattern=[[-1, P]], channel_multiplier=1).then_inc(ident_ready, 1)

            def gathers(c, p, use, reuse):
                pool.wait_ge(index_ready[p], (use + 1) * 16)
                for k, (h, g) in enumerate(SLOTS):
                    if reuse:
                        pool.wait_ge(fill_full, (c - 1) * N_FILLS + k + 1)
                        settle(pool)
                    for j, f in enumerate(SLOT_FEATURES[g]):
                        pool.indirect_dma_start(
                            rows[k][:, j * DIM:(j + 1) * DIM], None, tables[f],
                            bass.IndirectOffsetOnAxis(index[p][:, h, f:f + 1], 0)).then_inc(rows_in[k], 16)

            gathers(0, 0, 0, False)
            gathers(1, 1, 0, True)
            with pool.Fori(0, N_CHUNKS // 2 - 1) as i:
                gathers(i * 2 + 2, 0, i + 1, True)
                gathers(i * 2 + 3, 1, i + 1, True)

        @block.tensor
        def _(pe):
            pe.wait_ge(ident_ready, 1)

            def fill(c, k, lead):
                h, g = SLOTS[k]
                pe.wait_ge(rows_in[k], (c + 1) * 16 * len(SLOT_FEATURES[g]))
                if not lead or k >= 2:
                    pe.wait_ge(fill_out, c * N_FILLS + k - 1)
                for j in range(len(SLOT_FEATURES[g])):
                    last = nc.tensor.transpose(fill_ps[k % 2][:, j * P:(j + 1) * P],
                                               rows[k][:, j * DIM:(j + 1) * DIM], identity[:, :])
                last.then_inc(fill_full, 1)

            def step(c, p, use, with_fill, with_mlp, lead):
                pe.wait_ge(fill_out, (c + 1) * N_FILLS)
                for what, b in step_order(with_fill, with_mlp):
                    if what == "gram":
                        if not lead or b >= 2:
                            pe.wait_ge(gram_out_act, c * N_GRAMS + b - 1)
                            pe.wait_ge(gram_out_dve, c * N_GRAMS + b - 1)
                        for t in range(T_PER_BANK):
                            group = emb[p][:, b * T_PER_BANK + t, :, :]
                            last = nc.tensor.matmul(gram_ps[b % 2][:, t * COLS:(t + 1) * COLS],
                                                    group.rearrange("d q c -> d (q c)"), group[:, :, 0:PAIR_USED],
                                                    start=True, stop=True)
                        last.then_inc(gram_full, 1)
                    elif what == "fill":
                        fill(c + 1, b, False)
                    elif what == "layer1":
                        layer1(c - 1, 1 - p, use)
                    elif what == "layer2":
                        layer2(c - 1)
                    else:
                        layer3(c - 1)

            def layer1(c, p, uses):
                pe.wait_ge(z_ready[p], uses * 16 * Z_READS)
                for o in range(o1_tiles):
                    for k in range(3):
                        last = nc.tensor.matmul(h1_ps[o // 2][:, (o % 2) * CHUNK:(o % 2 + 1) * CHUNK],
                                                w1_sb[0:K_ROWS[k], k, o * P:(o + 1) * P], z[p][0:K_ROWS[k], k, :],
                                                start=(k == 0), stop=(k == 2))
                last.then_inc(l1_full, 1)

            def layer2(c):
                pe.wait_ge(h1_ready, c + 1)
                for o in range(o2_tiles):
                    for k in range(o1_tiles):
                        last = nc.tensor.matmul(h2_ps[:, o * CHUNK:(o + 1) * CHUNK],
                                                w2_sb[:, k, o * P:(o + 1) * P], h1[:, k, :],
                                                start=(k == 0), stop=(k == o1_tiles - 1))
                last.then_inc(l2_full, 1)

            def layer3(c):
                pe.wait_ge(h2_ready, c + 1)
                for k in range(o2_tiles):
                    last = nc.tensor.matmul(y_ps[0:1, 0:CHUNK], w3_sb[:, k:k + 1], h2[:, k, :],
                                            start=(k == 0), stop=(k == o2_tiles - 1))
                last.then_inc(l3_full, 1)

            for k in range(N_FILLS):
                fill(0, k, True)
            pe.wait_ge(pad_ready, 1)
            step(0, 0, 0, True, False, True)
            pe.wait_ge(weights_in, 16 * N_WEIGHTS)
            with pe.Fori(0, N_CHUNKS // 2 - 1) as i:
                step(i * 2 + 1, 1, i + 1, True, True, False)
                step(i * 2 + 2, 0, i + 1, True, True, False)
            step(N_CHUNKS - 1, 1, N_CHUNKS // 2, False, True, False)
            layer1(N_CHUNKS - 1, 1, N_CHUNKS // 2)
            layer2(N_CHUNKS - 1)
            layer3(N_CHUNKS - 1)

        @block.scalar
        def _(act):
            def fill_copy(c, p, k):
                h, g = SLOTS[k]
                f0, nf = SLOT_FEATURES[g][0], len(SLOT_FEATURES[g])
                act.wait_ge(fill_full, c * N_FILLS + k + 1)
                dst = emb[p][:, :, h, 0:PAIR_USED].rearrange("d t (s f) -> d f s t", f=FEATURES)
                nc.scalar.activation(dst[:, f0:f0 + nf, :, :],
                                     fill_ps[k % 2][:, 0:nf * P].rearrange("d (f s t) -> d f s t", f=nf, s=2),
                                     ACT.Copy).then_inc(fill_out, 1)

            def relu1(c):
                act.wait_ge(l1_full, c + 1)
                for o in range(o1_tiles):
                    last = nc.scalar.activation(h1[:, o, :], h1_ps[o // 2][:, (o % 2) * CHUNK:(o % 2 + 1) * CHUNK],
                                                ACT.Relu, bias=b1_sb[:, o:o + 1])
                last.then_inc(h1_ready, 1)

            def relu2(c):
                act.wait_ge(l2_full, c + 1)
                for o in range(o2_tiles):
                    last = nc.scalar.activation(h2[:, o, :], h2_ps[:, o * CHUNK:(o + 1) * CHUNK],
                                                ACT.Relu, bias=b2_sb[:, o:o + 1])
                last.then_inc(h2_ready, 1)

            def copy_y(c, p, use, reuse):
                act.wait_ge(l3_full, c + 1)
                if reuse:
                    act.wait_ge(y_stored[p], use * 16)
                nc.scalar.activation(y_sb[p][:, :], y_ps[0:1, 0:CHUNK], ACT.Copy).then_inc(y_ready, 1)

            def step(c, p, use, with_fill, with_mlp, reuse_gram, reuse_y):
                if reuse_gram:
                    act.wait_ge(x_written[p], use * 16 * X_WRITES)
                for what, b in step_order(with_fill, with_mlp):
                    if what == "gram":
                        act.wait_ge(gram_full, c * N_GRAMS + b + 1)
                        nc.scalar.activation(gram_block(p, 0, b), gram_block_ps(0, b), ACT.Copy
                                             ).then_inc(gram_out_act, 1)
                    elif what == "fill":
                        fill_copy(c + 1, 1 - p, b)
                    elif what == "layer1":
                        relu1(c - 1)
                    elif what == "layer2":
                        relu2(c - 1)
                    else:
                        copy_y(c - 1, 1 - p, use - 1 + p if reuse_y else 0, reuse_y)

            for k in range(N_FILLS):
                fill_copy(0, 0, k)
            act.wait_ge(weights_in, 16 * N_WEIGHTS)
            step(0, 0, 0, True, False, False, False)
            step(1, 1, 0, True, True, False, False)
            step(2, 0, 1, True, True, True, False)
            with act.Fori(0, N_CHUNKS // 2 - 2) as i:
                step(i * 2 + 3, 1, i + 1, True, True, True, True)
                step(i * 2 + 4, 0, i + 2, True, True, True, True)
            step(N_CHUNKS - 1, 1, N_CHUNKS // 2 - 1, False, True, True, True)
            relu1(N_CHUNKS - 1)
            relu2(N_CHUNKS - 1)
            copy_y(N_CHUNKS - 1, 1, N_CHUNKS // 2 - 1, True)

        @block.vector
        def _(dve):
            for p in range(2):
                last = nc.vector.memset(emb[p][:, :, :, PAIR_USED:], 0.0)
            last.then_inc(pad_ready, 1)

            def step(c, p, use, reuse):
                if reuse:
                    dve.wait_ge(x_written[p], use * 16 * X_WRITES)
                for b in range(N_GRAMS):
                    dve.wait_ge(gram_full, c * N_GRAMS + b + 1)
                    nc.vector.tensor_copy(gram_block(p, 1, b), gram_block_ps(1, b)).then_inc(gram_out_dve, 1)

            step(0, 0, 0, False)
            step(1, 1, 0, False)
            with dve.Fori(0, N_CHUNKS // 2 - 1) as i:
                step(i * 2 + 2, 0, i + 1, True)
                step(i * 2 + 3, 1, i + 1, True)


def layer1_row_order():
    order, dense = [], FEATURES * (FEATURES - 1) // 2
    for k in range(3):
        for n in range(k * N_TILE, (k + 1) * N_TILE):
            for distance in range(1, DIST + 1):
                m = (n + distance) % FEATURES
                hi, lo = max(n, m), min(n, m)
                order.append(hi * (hi - 1) // 2 + lo)
        order += list(range(dense, dense + DENSE_ROWS[k]))
        dense += DENSE_ROWS[k]
    return order


def kernel(**inputs):
    import numpy as np
    import concourse.bacc as bacc
    from concourse.bass_utils import run_bass_kernel_spmd

    def columns(v):
        return np.ascontiguousarray(np.asarray(v).reshape(-1, P).T)

    nc = bacc.Bacc("TRN2", target_bir_lowering=False, num_devices=1)
    arrays = {
        "dense_t": np.ascontiguousarray(np.asarray(inputs["dense_ctx"]).T),
        "ids": np.asarray(inputs["ids"]),
        "w1": np.ascontiguousarray(np.asarray(inputs["W_top1"])[layer1_row_order()]),
        "b1": columns(inputs["b_top1"]),
        "w2": np.asarray(inputs["W_top2"]),
        "b2": columns(inputs["b_top2"]),
        "w3": columns(inputs["W_top3"]),
    }
    for f in range(FEATURES):
        arrays[f"tbl_{f}"] = np.asarray(inputs[f"tbl_{f}"])
    aps = {k: nc.dram_tensor(k, v.shape, mybir.dt.from_np(v.dtype), kind="ExternalInput").ap()
           for k, v in arrays.items()}
    y = nc.dram_tensor("y", (BATCH, 1), mybir.dt.float32, kind="ExternalOutput").ap()
    dlrm_tower(nc, aps["dense_t"], aps["ids"], [aps[f"tbl_{f}"] for f in range(FEATURES)],
               aps["w1"], aps["b1"], aps["w2"], aps["b2"], aps["w3"], y)
    result = run_bass_kernel_spmd(nc, [arrays], core_ids=[0])
    return result.results[0]["y"]
```

```python
import concourse.bass as bass
from concourse import mybir
from contextlib import ExitStack

BATCH = 2048
FEATURES = 27
TABLE_ROWS = [125000, 12500, 12500, 1250, 1000, 1000, 12500, 1000, 12500, 12500, 1250, 1000, 1250, 1000, 1250, 12500,
              1000, 12500, 1000, 1250, 1250, 1000, 1000, 1000, 1250, 1000, 1000]
DIM = 128
DENSE = 16
HIDDEN1 = 512
HIDDEN2 = 256
P = 128

N_LOOKUP = 8
LOOKUP_ROWS = min(TABLE_ROWS)
LOOKUP = [f for f in range(FEATURES) if TABLE_ROWS[f] == LOOKUP_ROWS][:N_LOOKUP]
GATHER = [f for f in range(FEATURES) if f not in LOOKUP]
PART_ROWS = 8
LOOKUP_PARTS = LOOKUP_ROWS // PART_ROWS
ORDER = GATHER + LOOKUP

CHUNK = 256
N_CHUNKS = BATCH // CHUNK
GROUP = 4
LANE = CHUNK // GROUP
HALVES = CHUNK // P
COLS = GROUP * FEATURES
PAIRS = 2
PAIR_USED = GROUP // PAIRS * FEATURES
PAIR_COLS = 64
USED_COLS = PAIR_COLS + PAIR_USED

DIST = (FEATURES - 1) // 2
N_TILE = FEATURES // 3
PAIR_ROWS = N_TILE * DIST
DENSE_ROWS = (P - PAIR_ROWS, DENSE - (P - PAIR_ROWS), 0)
K_ROWS = tuple(PAIR_ROWS + d for d in DENSE_ROWS)

F_PER_SLOT = 4
SLOTS = [list(range(f, min(f + F_PER_SLOT, len(GATHER)))) for f in range(0, len(GATHER), F_PER_SLOT)]
N_GATHERS = HALVES * len(SLOTS)
T_PER_BANK = 4
N_GRAMS = LANE // T_PER_BANK
X_ROWS = FEATURES + DIST

UNIT_ROWS = 4
UNITS_PER_TABLE = PART_ROWS // UNIT_ROWS
N_UNITS = N_LOOKUP * UNITS_PER_TABLE
UNIT_RING = 4
LOOKUP_BANKS = 2
GATHER_BANKS = 2
STAGES = 4
FIRST_RATIO = 1.4
TABLES_AHEAD = 2


def first_order():
    order, gathers = [], 0
    for k in range(2 * N_LOOKUP):
        order.append((("lookup0", "lookup1")[k // N_LOOKUP], k % N_LOOKUP))
        while gathers < N_GATHERS and (gathers + 2) * FIRST_RATIO <= k + 1:
            order.append(("gather", gathers))
            gathers += 1
    return order + [("gather", k) for k in range(gathers, N_GATHERS)]


def step_order(with_gather, with_lookup):
    order = []
    gathers = iter(range(N_GATHERS))

    def gather():
        k = next(gathers, None)
        if with_gather and k is not None:
            order.append(("gather", k))

    for b in range(N_GRAMS):
        order.append(("gram", b))
        if b % 5 == 4:
            gather()
    mlp = {N_LOOKUP - 3: "layer1", N_LOOKUP - 2: "layer2", N_LOOKUP - 1: "layer3"}
    for k in range(N_LOOKUP):
        if with_lookup:
            order.append(("lookup", k))
        if k in mlp:
            order.append((mlp[k], 0))
        gather()
    return order


def dlrm_tower(nc, dense_t, ids, lookup_ids, tables, w1, b1, w2, b2, w3, y_out):
    fp32, fp32r, i32 = mybir.dt.float32, mybir.dt.float32r, mybir.dt.int32
    ALU, ACT = mybir.AluOpType, mybir.ActivationFunctionType
    o1_tiles, o2_tiles = HIDDEN1 // P, HIDDEN2 // P

    with ExitStack() as ctx:
        def sbuf(name, shape, dt=fp32):
            return ctx.enter_context(nc.sbuf_tensor(name, shape, dt))

        def psum(name):
            return ctx.enter_context(nc.psum_tensor(name, [P, 512], fp32))

        def semaphore(name):
            return ctx.enter_context(nc.semaphore(name))

        x_dram = nc.dram_tensor("gram_dram", [X_ROWS, FEATURES, GROUP, LANE], fp32, kind="Internal").ap()

        identity = sbuf("identity", [P, P])
        index = [sbuf(f"index{p}", [P, HALVES, FEATURES], i32) for p in range(2)]
        rows = [sbuf(f"rows{g}", [P, len(SLOTS[g]) * DIM]) for g in range(len(SLOTS))]
        table_hi = sbuf("table_hi", [LOOKUP_PARTS, N_LOOKUP, PART_ROWS, DIM], fp32r)
        table_lo = sbuf("table_lo", [LOOKUP_PARTS, N_LOOKUP, PART_ROWS, DIM], fp32r)
        row_number_int = sbuf("row_number_int", [P, PART_ROWS], i32)
        row_number = sbuf("row_number", [P, PART_ROWS])
        ids_all = sbuf("ids_all", [P, N_LOOKUP, CHUNK], i32)
        one_hot = [sbuf(f"one_hot{i}", [LOOKUP_PARTS, UNIT_ROWS, CHUNK], fp32r) for i in range(UNIT_RING)]
        emb = [sbuf(f"emb{p}", [P, LANE, PAIRS, PAIR_COLS]) for p in range(2)]
        gram = sbuf("gram", [P, PAIR_USED, LANE])
        z = sbuf("z", [P, 3, CHUNK])
        w1_sb = sbuf("w1_sb", [P, 3, HIDDEN1])
        w2_sb = sbuf("w2_sb", [P, o1_tiles, HIDDEN2])
        w3_sb = sbuf("w3_sb", [P, o2_tiles])
        b1_sb = sbuf("b1_sb", [P, o1_tiles])
        b2_sb = sbuf("b2_sb", [P, o2_tiles])
        h1 = sbuf("h1", [P, o1_tiles, CHUNK])
        h2 = sbuf("h2", [P, o2_tiles, CHUNK])
        y_sb = sbuf("y_sb", [1, CHUNK])

        gather_ps = [psum(f"gather_ps{i}") for i in range(GATHER_BANKS)]
        lookup_ps = [psum(f"lookup_ps{i}")[:, 0:CHUNK] for i in range(LOOKUP_BANKS)]
        gram_ps = [psum(f"gram_ps{i}") for i in range(2)]
        h1_ps = [psum(f"h1_ps{i}") for i in range(2)]
        h2_ps = h1_ps[1]
        y_ps = h1_ps[0][0:1, 0:CHUNK]

        weights_in = semaphore("weights_in")
        ident_zero = semaphore("ident_zero")
        consts_ready = semaphore("consts_ready")
        row_number_ready = semaphore("row_number_ready")
        stage_in = [semaphore(f"stage_in{i}") for i in range(STAGES)]
        table_hi_ready = semaphore("table_hi_ready")
        table_lo_ready = semaphore("table_lo_ready")
        pad_ready = semaphore("pad_ready")
        index_ready = [semaphore(f"index_ready{p}") for p in range(2)]
        rows_in = [semaphore(f"rows_in{g}") for g in range(len(SLOTS))]
        transposed = semaphore("transposed")
        gather_out = semaphore("gather_out")
        ids_ready = semaphore("ids_ready")
        unit_ready = semaphore("unit_ready")
        unit_free = semaphore("unit_free")
        lookup_out = semaphore("lookup_out")
        gram_full = semaphore("gram_full")
        gram_out_act = semaphore("gram_out_act")
        gram_out_dve = semaphore("gram_out_dve")
        x_written = semaphore("x_written")
        z_ready = semaphore("z_ready")
        l1_full = semaphore("l1_full")
        h1_ready = semaphore("h1_ready")
        l2_full = semaphore("l2_full")
        h2_ready = semaphore("h2_ready")
        l3_full = semaphore("l3_full")
        y_ready = semaphore("y_ready")
        y_stored = semaphore("y_stored")
        sp_passed = semaphore("sp_passed")
        pool_passed = semaphore("pool_passed")

        ROWS_FREE = len(SLOTS)
        GATHER_FREE = GATHER_BANKS
        LOOKUP_FREE = LOOKUP_BANKS
        GRAM_FREE = 2
        DMA_FREE = 16
        N_WEIGHTS = 7
        X_WRITES = 16 * 2 * GROUP
        Z_READS = 16 * 5

        def settle(engine):
            engine.sem_inc(sp_passed if engine is nc.sync else pool_passed, 1)

        def gram_block(q, b):
            return gram[64 * q:64 * q + PAIR_USED, :, b * T_PER_BANK:(b + 1) * T_PER_BANK]

        def gram_block_ps(q, b):
            src = gram_ps[b % 2][64 * q:64 * q + PAIR_USED, 0:T_PER_BANK * COLS]
            return src.rearrange("m (t c) -> m c t", c=COLS)[:, q * PAIR_USED:(q + 1) * PAIR_USED, :]

        def stage(i):
            flat = emb[1][:, :, :, :].rearrange("p t q c -> p (t q c)")
            return flat[0:LOOKUP_PARTS, i * PART_ROWS * DIM:(i + 1) * PART_ROWS * DIM]

        block = ctx.enter_context(nc.Block())

        @block.sync
        def _(sp):
            sp.sem_inc(x_written, DMA_FREE)
            sp.sem_inc(z_ready, DMA_FREE)
            sp.sem_inc(y_stored, DMA_FREE)

            def load_index(c, p):
                src = ids[bass.ds(c * CHUNK, CHUNK), :].rearrange("(h p) f -> p h f", p=P)
                sp.dma_start(index[p][:, :, :], src).then_inc(index_ready[p], 16)

            def load_ids(c):
                src = lookup_ids[:, bass.ds(c * CHUNK, CHUNK)]
                sp.dma_start(ids_all[:, :, :], src.partition_broadcast(P)).then_inc(ids_ready, 16)

            def load_table(k):
                src = tables[LOOKUP[k]].rearrange("(p r) d -> p (r d)", r=PART_ROWS)
                sp.dma_start(stage(k % STAGES), src).then_inc(stage_in[k % STAGES], 16)

            load_index(0, 0)
            load_ids(0)
            for k in range(STAGES):
                load_table(k)
            load_index(1, 1)
            for k in range(STAGES, N_LOOKUP):
                sp.wait_ge(table_hi_ready, k - STAGES + 1)
                sp.wait_ge(table_lo_ready, k - STAGES + 1)
                load_table(k)
            k0 = 0
            for k in range(3):
                sp.dma_start(w1_sb[0:K_ROWS[k], k, :], w1[k0:k0 + K_ROWS[k], :]).then_inc(weights_in, 16)
                k0 += K_ROWS[k]
            sp.dma_start(w2_sb[:, :, :], w2.rearrange("(k p) o -> p k o", p=P)).then_inc(weights_in, 16)
            sp.dma_start(w3_sb[:, :], w3).then_inc(weights_in, 16)
            sp.dma_start(b1_sb[:, :], b1).then_inc(weights_in, 16)
            sp.dma_start(b2_sb[:, :], b2).then_inc(weights_in, 16)
            sp.wait_ge(unit_ready, N_UNITS)
            load_ids(1)

            def step(c, p, prefetch):
                if prefetch:
                    sp.wait_ge(unit_ready, (c + 2) * N_UNITS)
                    settle(sp)
                    load_ids(c + 2)
                    sp.wait_ge(transposed, (c + 1) * N_GATHERS + ROWS_FREE)
                    settle(sp)
                    load_index(c + 2, p)
                sp.wait_ge(gram_out_act, (c + 1) * N_GRAMS + GRAM_FREE)
                sp.wait_ge(gram_out_dve, (c + 1) * N_GRAMS + GRAM_FREE)
                settle(sp)
                sp.wait_ge(z_ready, c * Z_READS + DMA_FREE)
                settle(sp)
                for s in range(GROUP):
                    r = 64 * (s // 2) + FEATURES * (s % 2)
                    cols = slice(FEATURES * (s % 2), FEATURES * (s % 2 + 1))
                    sp.dma_start(x_dram[0:FEATURES, :, s, :], gram[r:r + FEATURES, cols, :]
                                 ).then_inc(x_written, 16)
                    sp.dma_start(x_dram[FEATURES:X_ROWS, :, s, :], gram[r:r + DIST, cols, :]
                                 ).then_inc(x_written, 16)
                sp.wait_ge(l1_full, c + 1)
                sp.wait_ge(x_written, (c + 1) * X_WRITES + DMA_FREE)
                settle(sp)
                row = FEATURES * CHUNK
                for k in range(3):
                    n0 = k * N_TILE
                    src = bass.AP(x_dram.tensor, (n0 + 1) * row + n0 * CHUNK,
                                  [[row + CHUNK, N_TILE], [row, DIST], [1, CHUNK]])
                    sp.dma_start(z[0:PAIR_ROWS, k, :], src).then_inc(z_ready, 16)
                sp.dma_start(z[PAIR_ROWS:K_ROWS[0], 0, :],
                             dense_t[0:DENSE_ROWS[0], bass.ds(c * CHUNK, CHUNK)]).then_inc(z_ready, 16)
                sp.dma_start(z[PAIR_ROWS:K_ROWS[1], 1, :],
                             dense_t[DENSE_ROWS[0]:DENSE, bass.ds(c * CHUNK, CHUNK)]).then_inc(z_ready, 16)
                sp.wait_ge(y_ready, c + 2)
                settle(sp)
                sp.dma_start(y_out[bass.ds(c * CHUNK, CHUNK), :].rearrange("b o -> o b"),
                             y_sb[:, :]).then_inc(y_stored, 16)

            with sp.Fori(0, N_CHUNKS // 2 - 1) as i:
                step(i * 2, 0, True)
                step(i * 2 + 1, 1, True)
            step(N_CHUNKS - 2, 0, False)
            step(N_CHUNKS - 1, 1, False)
            sp.wait_ge(y_stored, 16 * N_CHUNKS + DMA_FREE)

        @block.gpsimd
        def _(pool):
            def gathers(c, p, use):
                pool.wait_ge(index_ready[p], (use + 1) * 16)
                settle(pool)
                for k in range(N_GATHERS):
                    h, g = divmod(k, len(SLOTS))
                    pool.wait_ge(transposed, c * N_GATHERS + k + 1)
                    settle(pool)
                    for j, n in enumerate(SLOTS[g]):
                        f = ORDER[n]
                        pool.indirect_dma_start(
                            rows[g][:, j * DIM:(j + 1) * DIM], None, tables[f],
                            bass.IndirectOffsetOnAxis(index[p][:, h, f:f + 1], 0)).then_inc(rows_in[g], 16)

            nc.gpsimd.iota(row_number_int[:, :], [[1, PART_ROWS]], base=0, channel_multiplier=PART_ROWS
                           ).then_inc(consts_ready, 1)
            nc.gpsimd.memset(identity[:, :], 0.0).then_inc(ident_zero, 1)
            pool.wait_ge(ident_zero, 1)
            nc.gpsimd.affine_select(out=identity[:, :], in_=identity[:, :], compare_op=ALU.not_equal, fill=1.0,
                                    base=0, pattern=[[-1, P]], channel_multiplier=1).then_inc(consts_ready, 1)
            with pool.Fori(0, N_CHUNKS // 2) as i:
                gathers(i * 2, 0, i)
                gathers(i * 2 + 1, 1, i)

        @block.tensor
        def _(pe):
            pe.sem_inc(transposed, ROWS_FREE)
            pe.sem_inc(unit_free, UNIT_RING)
            pe.sem_inc(l1_full, 1)

            def gather(c, k):
                g = k % len(SLOTS)
                pe.wait_ge(rows_in[g], (c * HALVES + k // len(SLOTS) + 1) * 16 * len(SLOTS[g]))
                pe.wait_ge(gather_out, c * N_GATHERS + k + 1)
                for j in range(len(SLOTS[g])):
                    last = nc.tensor.transpose(gather_ps[k % GATHER_BANKS][:, j * P:(j + 1) * P],
                                               rows[g][:, j * DIM:(j + 1) * DIM], identity[:, :])
                last.then_inc(transposed, 1)

            def lookup(c, k):
                pe.wait_ge(lookup_out, c * N_LOOKUP + k + 1)
                for u in range(UNITS_PER_TABLE):
                    unit = k * UNITS_PER_TABLE + u
                    pe.wait_ge(unit_ready, c * N_UNITS + unit + 1)
                    for r in range(UNIT_ROWS):
                        row = u * UNIT_ROWS + r
                        for table in (table_hi, table_lo):
                            last = nc.tensor.matmul(lookup_ps[k % LOOKUP_BANKS], table[:, k, row, :],
                                                    one_hot[unit % UNIT_RING][:, r, :],
                                                    start=(row == 0 and table is table_hi),
                                                    stop=(row == PART_ROWS - 1 and table is table_lo))
                    last.then_inc(unit_free, 1)

            def gram_bank(c, p, b):
                pe.wait_ge(gram_out_act, c * N_GRAMS + b + 1)
                pe.wait_ge(gram_out_dve, c * N_GRAMS + b + 1)
                for t in range(T_PER_BANK):
                    group = emb[p][:, b * T_PER_BANK + t, :, :]
                    last = nc.tensor.matmul(gram_ps[b % 2][0:USED_COLS, t * COLS:(t + 1) * COLS],
                                            group.rearrange("d q c -> d (q c)")[:, 0:USED_COLS],
                                            group[:, :, 0:PAIR_USED],
                                            start=True, stop=True)
                last.then_inc(gram_full, 1)

            def layer1(c):
                pe.wait_ge(z_ready, (c + 1) * Z_READS + DMA_FREE)
                pe.wait_ge(y_ready, c + 1)
                for o in range(o1_tiles):
                    for k in range(3):
                        last = nc.tensor.matmul(h1_ps[o // 2][:, (o % 2) * CHUNK:(o % 2 + 1) * CHUNK],
                                                w1_sb[0:K_ROWS[k], k, o * P:(o + 1) * P], z[0:K_ROWS[k], k, :],
                                                start=(k == 0), stop=(k == 2))
                last.then_inc(l1_full, 1)

            def layer2(c):
                pe.wait_ge(h1_ready, c + 1)
                for o in range(o2_tiles):
                    for k in range(o1_tiles):
                        last = nc.tensor.matmul(h2_ps[:, o * CHUNK:(o + 1) * CHUNK],
                                                w2_sb[:, k, o * P:(o + 1) * P], h1[:, k, :],
                                                start=(k == 0), stop=(k == o1_tiles - 1))
                last.then_inc(l2_full, 1)

            def layer3(c):
                pe.wait_ge(h2_ready, c + 1)
                for k in range(o2_tiles):
                    last = nc.tensor.matmul(y_ps, w3_sb[:, k:k + 1], h2[:, k, :],
                                            start=(k == 0), stop=(k == o2_tiles - 1))
                last.then_inc(l3_full, 1)

            def step(c, p, with_gather, with_lookup):
                pe.wait_ge(gather_out, (c + 1) * N_GATHERS + GATHER_FREE)
                pe.wait_ge(lookup_out, (c + 1) * N_LOOKUP + LOOKUP_FREE)
                for what, k in step_order(with_gather, with_lookup):
                    if what == "gram":
                        gram_bank(c, p, k)
                    elif what == "gather":
                        gather(c + 1, k)
                    elif what == "lookup":
                        lookup(c + 2, k)
                    elif what == "layer1":
                        layer1(c)
                    elif what == "layer2":
                        layer2(c)
                    else:
                        layer3(c)

            pe.wait_ge(consts_ready, 2)
            for what, k in first_order():
                if what == "gather":
                    gather(0, k)
                elif what == "lookup0":
                    pe.wait_ge(table_hi_ready, k + 1)
                    pe.wait_ge(table_lo_ready, k + 1)
                    lookup(0, k)
                else:
                    lookup(1, k)
            pe.wait_ge(pad_ready, 2)
            pe.wait_ge(weights_in, 16 * N_WEIGHTS)
            with pe.Fori(0, N_CHUNKS // 2 - 1) as i:
                step(i * 2, 0, True, True)
                step(i * 2 + 1, 1, True, True)
            step(N_CHUNKS - 2, 0, True, False)
            step(N_CHUNKS - 1, 1, False, False)

        @block.scalar
        def _(act):
            act.sem_inc(gather_out, GATHER_FREE)
            act.sem_inc(lookup_out, LOOKUP_FREE)
            act.sem_inc(gram_out_act, GRAM_FREE)
            act.sem_inc(y_ready, 1)

            def copy_gather(c, p, k):
                h, g = divmod(k, len(SLOTS))
                n0, n = SLOTS[g][0], len(SLOTS[g])
                act.wait_ge(transposed, c * N_GATHERS + k + 1 + ROWS_FREE)
                dst = emb[p][:, :, h, 0:PAIR_USED].rearrange("d t (s f) -> d f s t", f=FEATURES)
                nc.scalar.activation(dst[:, n0:n0 + n, :, :],
                                     gather_ps[k % GATHER_BANKS][:, 0:n * P].rearrange("d (f s t) -> d f s t", f=n, s=2),
                                     ACT.Copy).then_inc(gather_out, 1)

            def copy_lookup(c, p, k):
                act.wait_ge(unit_free, c * N_UNITS + (k + 1) * UNITS_PER_TABLE + UNIT_RING)
                dst = emb[p][:, :, :, 0:PAIR_USED].rearrange("d t q (s f) -> d f q s t", f=FEATURES)
                nc.scalar.activation(dst[:, len(GATHER) + k, :, :, :],
                                     lookup_ps[k % LOOKUP_BANKS].rearrange("d (q s t) -> d q s t", q=PAIRS, t=LANE),
                                     ACT.Copy).then_inc(lookup_out, 1)

            def relu1(c):
                act.wait_ge(l1_full, c + 2)
                for o in range(o1_tiles):
                    last = nc.scalar.activation(h1[:, o, :], h1_ps[o // 2][:, (o % 2) * CHUNK:(o % 2 + 1) * CHUNK],
                                                ACT.Relu, bias=b1_sb[:, o:o + 1])
                last.then_inc(h1_ready, 1)

            def relu2(c):
                act.wait_ge(l2_full, c + 1)
                for o in range(o2_tiles):
                    last = nc.scalar.activation(h2[:, o, :], h2_ps[:, o * CHUNK:(o + 1) * CHUNK],
                                                ACT.Relu, bias=b2_sb[:, o:o + 1])
                last.then_inc(h2_ready, 1)

            def copy_y(c):
                act.wait_ge(l3_full, c + 1)
                act.wait_ge(y_stored, c * 16 + DMA_FREE)
                nc.scalar.activation(y_sb[:, :], y_ps, ACT.Copy).then_inc(y_ready, 1)

            def step(c, p, with_gather, with_lookup):
                act.wait_ge(x_written, c * X_WRITES + DMA_FREE)
                for what, k in step_order(with_gather, with_lookup):
                    if what == "gram":
                        act.wait_ge(gram_full, c * N_GRAMS + k + 1)
                        nc.scalar.activation(gram_block(0, k), gram_block_ps(0, k), ACT.Copy
                                             ).then_inc(gram_out_act, 1)
                    elif what == "gather":
                        copy_gather(c + 1, 1 - p, k)
                    elif what == "lookup":
                        copy_lookup(c + 2, p, k)
                    elif what == "layer1":
                        relu1(c)
                    elif what == "layer2":
                        relu2(c)
                    else:
                        copy_y(c)

            def table_high(k):
                act.wait_ge(stage_in[k % STAGES], (k // STAGES + 1) * 16)
                nc.scalar.activation(table_hi[:, k, :, :].rearrange("p r d -> p (r d)"), stage(k % STAGES), ACT.Copy
                                     ).then_inc(table_hi_ready, 1)

            for what, k in first_order():
                if what == "gather":
                    copy_gather(0, 0, k)
                elif what == "lookup0":
                    for n in range(k + TABLES_AHEAD if k else 0, min(k + 1 + TABLES_AHEAD, N_LOOKUP)):
                        table_high(n)
                    copy_lookup(0, 0, k)
                else:
                    act.wait_ge(table_lo_ready, N_LOOKUP)
                    copy_lookup(1, 1, k)
            act.wait_ge(weights_in, 16 * N_WEIGHTS)
            with act.Fori(0, N_CHUNKS // 2 - 1) as i:
                step(i * 2, 0, True, True)
                step(i * 2 + 1, 1, True, True)
            step(N_CHUNKS - 2, 0, True, False)
            step(N_CHUNKS - 1, 1, False, False)

        @block.vector
        def _(dve):
            dve.sem_inc(gram_out_dve, GRAM_FREE)

            def unit(c, u):
                k, u0 = divmod(u, UNITS_PER_TABLE)
                dve.wait_ge(unit_free, c * N_UNITS + u + 1)
                for r in range(UNIT_ROWS):
                    row = u0 * UNIT_ROWS + r
                    last = nc.vector.tensor_scalar(one_hot[u % UNIT_RING][:, r, :], ids_all[0:LOOKUP_PARTS, k, :],
                                                   row_number[0:LOOKUP_PARTS, row:row + 1], None, ALU.is_equal)
                last.then_inc(unit_ready, 1)

            nc.vector.memset(emb[0][:, :, :, PAIR_USED:], 0.0).then_inc(pad_ready, 1)
            dve.wait_ge(consts_ready, 1)
            nc.vector.tensor_copy(row_number[:, :], row_number_int[:, :]).then_inc(row_number_ready, 1)
            dve.wait_ge(row_number_ready, 1)
            dve.wait_ge(ids_ready, 16)
            for k in range(N_LOOKUP):
                dve.wait_ge(table_hi_ready, k + 1)
                nc.vector.tensor_tensor(table_lo[:, k, :, :].rearrange("p r d -> p (r d)"), stage(k % STAGES),
                                        table_hi[:, k, :, :].rearrange("p r d -> p (r d)").bitcast(fp32),
                                        ALU.subtract).then_inc(table_lo_ready, 1)
                for u in range(UNITS_PER_TABLE):
                    unit(0, k * UNITS_PER_TABLE + u)
            dve.wait_ge(table_lo_ready, N_LOOKUP)
            nc.vector.memset(emb[1][:, :, :, PAIR_USED:], 0.0).then_inc(pad_ready, 1)
            dve.wait_ge(ids_ready, 2 * 16)
            for u in range(N_UNITS):
                unit(1, u)

            def step(c, with_lookup):
                dve.wait_ge(x_written, c * X_WRITES + DMA_FREE)
                for b in range(N_GRAMS):
                    dve.wait_ge(gram_full, c * N_GRAMS + b + 1)
                    nc.vector.tensor_copy(gram_block(1, b), gram_block_ps(1, b)).then_inc(gram_out_dve, 1)
                    if with_lookup and b >= N_GRAMS - UNIT_RING:
                        if b == N_GRAMS - UNIT_RING:
                            dve.wait_ge(ids_ready, (c + 3) * 16)
                        unit(c + 2, b - (N_GRAMS - UNIT_RING))
                if with_lookup:
                    for u in range(UNIT_RING, N_UNITS):
                        unit(c + 2, u)

            with dve.Fori(0, N_CHUNKS // 2 - 1) as i:
                step(i * 2, True)
                step(i * 2 + 1, True)
            step(N_CHUNKS - 2, False)
            step(N_CHUNKS - 1, False)


def layer1_row_order():
    order, dense = [], FEATURES * (FEATURES - 1) // 2
    for k in range(3):
        for n in range(k * N_TILE, (k + 1) * N_TILE):
            for distance in range(1, DIST + 1):
                m = (n + distance) % FEATURES
                hi, lo = max(ORDER[n], ORDER[m]), min(ORDER[n], ORDER[m])
                order.append(hi * (hi - 1) // 2 + lo)
        order += list(range(dense, dense + DENSE_ROWS[k]))
        dense += DENSE_ROWS[k]
    return order


def kernel(**inputs):
    import numpy as np
    import concourse.bacc as bacc
    from concourse.bass_utils import run_bass_kernel_spmd

    def columns(v):
        return np.ascontiguousarray(np.asarray(v).reshape(-1, P).T)

    nc = bacc.Bacc("TRN2", target_bir_lowering=False, num_devices=1)
    arrays = {
        "dense_t": np.ascontiguousarray(np.asarray(inputs["dense_ctx"]).T),
        "ids": np.asarray(inputs["ids"]),
        "lookup_ids": np.ascontiguousarray(np.asarray(inputs["ids"]).T[LOOKUP]),
        "w1": np.ascontiguousarray(np.asarray(inputs["W_top1"])[layer1_row_order()]),
        "b1": columns(inputs["b_top1"]),
        "w2": np.asarray(inputs["W_top2"]),
        "b2": columns(inputs["b_top2"]),
        "w3": columns(inputs["W_top3"]),
    }
    for f in range(FEATURES):
        arrays[f"tbl_{f}"] = np.asarray(inputs[f"tbl_{f}"])
    aps = {k: nc.dram_tensor(k, v.shape, mybir.dt.from_np(v.dtype), kind="ExternalInput").ap()
           for k, v in arrays.items()}
    y = nc.dram_tensor("y", (BATCH, 1), mybir.dt.float32, kind="ExternalOutput").ap()
    dlrm_tower(nc, aps["dense_t"], aps["ids"], aps["lookup_ids"], [aps[f"tbl_{f}"] for f in range(FEATURES)],
               aps["w1"], aps["b1"], aps["w2"], aps["b2"], aps["w3"], y)
    result = run_bass_kernel_spmd(nc, [arrays], core_ids=[0])
    return result.results[0]["y"]
```

```python
import concourse.bass as bass
from concourse import mybir
from contextlib import ExitStack

BATCH = 2048
FEATURES = 27
TABLE_ROWS = [125000, 12500, 12500, 1250, 1000, 1000, 12500, 1000, 12500, 12500, 1250, 1000, 1250, 1000, 1250, 12500,
              1000, 12500, 1000, 1250, 1250, 1000, 1000, 1000, 1250, 1000, 1000]
DIM = 128
DENSE = 16
HIDDEN1 = 512
HIDDEN2 = 256
P = 128

N_LOOKUP = 8
LOOKUP_ROWS = min(TABLE_ROWS)
LOOKUP = [f for f in range(FEATURES) if TABLE_ROWS[f] == LOOKUP_ROWS][:N_LOOKUP]
GATHER = [f for f in range(FEATURES) if f not in LOOKUP]
PART_ROWS = 8
LOOKUP_PARTS = LOOKUP_ROWS // PART_ROWS
ORDER = GATHER + LOOKUP

CHUNK = 256
N_CHUNKS = BATCH // CHUNK
GROUP = 4
LANE = CHUNK // GROUP
HALVES = CHUNK // P
COLS = GROUP * FEATURES
QUAD = 32
HALF_LANE = LANE // HALVES
USED_COLS = (GROUP - 1) * QUAD + FEATURES

DIST = (FEATURES - 1) // 2
N_TILES = (9, 9, 8)
K_TILES = len(N_TILES)
PAIR_ROWS = N_TILES[0] * DIST
DENSE_ROWS = (P - PAIR_ROWS, DENSE - (P - PAIR_ROWS), 0)
K_ROWS = tuple(PAIR_ROWS + d for d in DENSE_ROWS)

F_PER_SLOT = 4
SLOTS = [list(range(f, min(f + F_PER_SLOT, len(GATHER)))) for f in range(0, len(GATHER), F_PER_SLOT)]
N_GATHERS = HALVES * len(SLOTS)
T_PER_BANK = 4
N_GRAMS = LANE // T_PER_BANK

UNIT_ROWS = 2
UNITS_PER_TABLE = PART_ROWS // UNIT_ROWS
N_UNITS = N_LOOKUP * UNITS_PER_TABLE
UNIT_RING = 8
ID_PARTS = 2
TABLES_PER_PART = N_LOOKUP // ID_PARTS
UNITS_PER_PART = N_UNITS // ID_PARTS

LOOKUP_BANKS = 2
GATHER_BANKS = 2
STAGES = 4
TABLES_AHEAD = 2

LAYERS = ("layer1", "layer2", "layer3")
EARLY_UNITS = 24
UNITS_PER_GATHER = 5
GATHERS_IN_GRAM = 4
SPLIT_AFTER = 19
LAYERS_AFTER = (22, 23)


def first_order():
    order, gathers = [], 0
    for k in range(N_UNITS + EARLY_UNITS):
        order.append(("unit", k // N_UNITS, k % N_UNITS))
        while gathers < N_GATHERS and (gathers + 1.5) * UNITS_PER_GATHER <= k + 1:
            order.append(("gather", 0, gathers))
            gathers += 1
    return order + [("gather", 0, k) for k in range(gathers, N_GATHERS)]


def gram_order(c, units, gathers):
    order, u, g = [], 0, 0
    for b in range(N_GRAMS):
        order.append(("gram", c, b))
        while (b + 1) * units >= (u + 1) * N_GRAMS:
            order.append(("unit", c + 1, EARLY_UNITS + u))
            u += 1
        if (b + 1) * (gathers + 1) >= (g + 1) * N_GRAMS and g < gathers:
            order.append(("gather", c + 1, g))
            g += 1
    return order


def step_order(c):
    order, g = gram_order(c, N_UNITS - EARLY_UNITS, GATHERS_IN_GRAM), GATHERS_IN_GRAM
    for u in range(EARLY_UNITS):
        order.append(("unit", c + 2, u))
        if (u + 1) * (N_GATHERS - GATHERS_IN_GRAM) >= (g - GATHERS_IN_GRAM + 1) * (EARLY_UNITS - 1) and g < N_GATHERS:
            order.append(("gather", c + 1, g))
            g += 1
        if u == SPLIT_AFTER:
            order.append(("split", c, None))
        if u in LAYERS_AFTER:
            order.append((LAYERS[LAYERS_AFTER.index(u)], c, None))
    return order + [("layer3", c, None)]


def last_order():
    c, half, slots = N_CHUNKS - 2, N_GRAMS // HALVES, len(SLOTS)
    order = gram_order(c, 0, 2)
    order += [("unit", c + 1, u) for u in range(EARLY_UNITS, N_UNITS)]
    order += [("gather", c + 1, k) for k in range(2, slots)]
    order += [("gram", c + 1, b) for b in range(half)]
    order.append(("split", c, None))
    order += [("gather", c + 1, k) for k in range(slots, N_GATHERS)]
    order += [("gram", c + 1, b) for b in range(half, N_GRAMS)]
    order += [(layer, c, None) for layer in LAYERS]
    return order + [(part, c + 1, None) for part in ("split",) + LAYERS]


def dlrm_tower(nc, dense_t, ids, lookup_ids, tables, w1, b1, w2, b2, w3, y_out):
    fp32, fp32r, i32 = mybir.dt.float32, mybir.dt.float32r, mybir.dt.int32
    ALU, ACT = mybir.AluOpType, mybir.ActivationFunctionType
    o1_tiles, o2_tiles = HIDDEN1 // P, HIDDEN2 // P
    LAYER_BANKS = 2
    TILES_PER_BANK = o1_tiles // LAYER_BANKS

    with ExitStack() as ctx:
        def sbuf(name, shape, dt=fp32):
            return ctx.enter_context(nc.sbuf_tensor(name, shape, dt))

        def psum(name):
            return ctx.enter_context(nc.psum_tensor(name, [P, 512], fp32))

        def semaphore(name):
            return ctx.enter_context(nc.semaphore(name))

        x_dram = nc.dram_tensor("gram_dram", [FEATURES, FEATURES, GROUP, LANE], fp32, kind="Internal").ap()

        identity = sbuf("identity", [P, P])
        index = [sbuf(f"index{p}", [P, HALVES, FEATURES], i32) for p in range(2)]
        rows = [sbuf(f"rows{g}", [P, len(SLOTS[g]) * DIM]) for g in range(len(SLOTS))]
        table_hi = sbuf("table_hi", [LOOKUP_PARTS, N_LOOKUP, PART_ROWS, DIM], fp32r)
        table_lo = sbuf("table_lo", [LOOKUP_PARTS, N_LOOKUP, PART_ROWS, DIM], fp32r)
        row_number_int = sbuf("row_number_int", [P, PART_ROWS], i32)
        row_number = sbuf("row_number", [P, PART_ROWS])
        ids_all = [sbuf(f"ids_all{part}", [P, TABLES_PER_PART, CHUNK], i32) for part in range(ID_PARTS)]
        one_hot = [sbuf(f"one_hot{i}", [LOOKUP_PARTS, UNIT_ROWS, CHUNK], fp32r) for i in range(UNIT_RING)]
        emb = [sbuf(f"emb{p}", [P, LANE, GROUP, QUAD]) for p in range(2)]
        gram = sbuf("gram", [GROUP * QUAD, FEATURES, LANE])
        z = sbuf("z", [P, K_TILES, CHUNK])
        z_hi = sbuf("z_hi", [P, K_TILES, CHUNK], fp32r)
        z_lo = sbuf("z_lo", [P, K_TILES, CHUNK], fp32r)
        w1_hi = sbuf("w1_hi", [P, K_TILES, HIDDEN1], fp32r)
        w1_lo = sbuf("w1_lo", [P, K_TILES, HIDDEN1], fp32r)
        w1_flat = gram[:, :, :].rearrange("p n t -> p (n t)")[:, 0:K_TILES * HIDDEN1]
        w1_sb = w1_flat.rearrange("p (k o) -> p k o", k=K_TILES)
        w2_sb = sbuf("w2_sb", [P, o1_tiles, HIDDEN2])
        w3_sb = sbuf("w3_sb", [P, o2_tiles])
        b1_sb = sbuf("b1_sb", [P, o1_tiles])
        b2_sb = sbuf("b2_sb", [P, o2_tiles])
        h1 = sbuf("h1", [P, o1_tiles, CHUNK])
        h2 = sbuf("h2", [P, o2_tiles, CHUNK])
        y_sb = sbuf("y_sb", [1, CHUNK])

        gather_ps = [psum(f"gather_ps{i}") for i in range(GATHER_BANKS)]
        lookup_ps = [psum(f"lookup_ps{i}")[:, 0:CHUNK] for i in range(LOOKUP_BANKS)]
        gram_ps = [psum(f"gram_ps{i}") for i in range(2)]
        layer_ps = [psum(f"layer_ps{i}") for i in range(LAYER_BANKS)]

        w1_in = semaphore("w1_in")
        weights_in = semaphore("weights_in")
        ident_zero = semaphore("ident_zero")
        consts_ready = semaphore("consts_ready")
        row_number_ready = semaphore("row_number_ready")
        stage_in = [semaphore(f"stage_in{i}") for i in range(STAGES)]
        table_hi_ready = semaphore("table_hi_ready")
        table_lo_ready = semaphore("table_lo_ready")
        pad_ready = semaphore("pad_ready")
        index_ready = [semaphore(f"index_ready{p}") for p in range(2)]
        rows_in = [semaphore(f"rows_in{g}") for g in range(len(SLOTS))]
        transposed = semaphore("transposed")
        gather_out = semaphore("gather_out")
        ids_ready = [semaphore(f"ids_ready{part}") for part in range(ID_PARTS)]
        unit_ready = semaphore("unit_ready")
        unit_free = semaphore("unit_free")
        lookup_out = semaphore("lookup_out")
        gram_full = semaphore("gram_full")
        gram_out_act = semaphore("gram_out_act")
        gram_out_dve = semaphore("gram_out_dve")
        x_written = semaphore("x_written")
        z_ready = semaphore("z_ready")
        z_cleared = semaphore("z_cleared")
        z_hi_ready = semaphore("z_hi_ready")
        z_split = semaphore("z_split")
        w1_hi_ready = semaphore("w1_hi_ready")
        w1_split = semaphore("w1_split")
        l1_full = semaphore("l1_full")
        h1_ready = semaphore("h1_ready")
        l2_full = semaphore("l2_full")
        h2_ready = semaphore("h2_ready")
        l3_full = semaphore("l3_full")
        y_ready = semaphore("y_ready")
        y_stored = semaphore("y_stored")
        sp_passed = semaphore("sp_passed")
        pool_passed = semaphore("pool_passed")
        act_passed = semaphore("act_passed")

        ROWS_FREE = len(SLOTS)
        GATHER_FREE = GATHER_BANKS
        LOOKUP_FREE = LOOKUP_BANKS
        GRAM_FREE = 2
        DMA_FREE = 16
        W1_LOADS = 16 * K_TILES
        WEIGHT_LOADS = 16 * 4
        X_WRITES = 16 * GROUP
        Z_READS = 16 * (K_TILES + 3)

        def settle(engine):
            passed = {nc.sync: sp_passed, nc.gpsimd: pool_passed, nc.scalar: act_passed}
            engine.sem_inc(passed[engine], 1)

        def copy_grams(copy, b, samples, done):
            for sample in samples:
                r = slice(QUAD * sample, QUAD * sample + FEATURES)
                src = gram_ps[b % 2][r, 0:T_PER_BANK * COLS].rearrange("m (t s n) -> m s n t", s=GROUP, n=FEATURES)
                last = copy(gram[r, :, b * T_PER_BANK:(b + 1) * T_PER_BANK], src[:, sample, :, :])
            last.then_inc(done, 1)

        def stage(i):
            flat = emb[1][:, :, :, :].rearrange("p t s f -> p (t s f)")
            return flat[0:LOOKUP_PARTS, i * PART_ROWS * DIM:(i + 1) * PART_ROWS * DIM]

        block = ctx.enter_context(nc.Block())

        @block.sync
        def _(sp):
            sp.sem_inc(x_written, DMA_FREE)
            sp.sem_inc(z_ready, DMA_FREE)

            def load_index(c, p):
                src = ids[bass.ds(c * CHUNK, CHUNK), :].rearrange("(h p) f -> p h f", p=P)
                sp.dma_start(index[p][:, :, :], src).then_inc(index_ready[p], 16)

            def load_ids(c, part):
                src = lookup_ids[part * TABLES_PER_PART:(part + 1) * TABLES_PER_PART, bass.ds(c * CHUNK, CHUNK)]
                sp.dma_start(ids_all[part][:, :, :], src.partition_broadcast(P)).then_inc(ids_ready[part], 16)

            def load_table(k):
                src = tables[LOOKUP[k]].rearrange("(p r) d -> p (r d)", r=PART_ROWS)
                sp.dma_start(stage(k % STAGES), src).then_inc(stage_in[k % STAGES], 16)

            load_index(0, 0)
            k0 = 0
            for k in range(K_TILES):
                sp.dma_start(w1_sb[0:K_ROWS[k], k, :], w1[k0:k0 + K_ROWS[k], :]).then_inc(w1_in, 16)
                k0 += K_ROWS[k]
            load_ids(0, 0)
            load_table(0)
            load_table(1)
            load_ids(0, 1)
            for k in range(2, STAGES):
                load_table(k)
            load_index(1, 1)
            for k in range(STAGES, N_LOOKUP):
                sp.wait_ge(table_hi_ready, k - STAGES + 1)
                sp.wait_ge(table_lo_ready, k - STAGES + 1)
                load_table(k)
            for part in range(ID_PARTS):
                sp.wait_ge(unit_ready, (part + 1) * UNITS_PER_PART)
                load_ids(1, part)
            sp.dma_start(w2_sb[:, :, :], w2.rearrange("(k p) o -> p k o", p=P)).then_inc(weights_in, 16)
            sp.dma_start(w3_sb[:, :], w3).then_inc(weights_in, 16)
            sp.dma_start(b1_sb[:, :], b1).then_inc(weights_in, 16)
            sp.dma_start(b2_sb[:, :], b2).then_inc(weights_in, 16)

            def prefetch(c, p):
                for part in range(ID_PARTS):
                    sp.wait_ge(unit_ready, (c - 1) * N_UNITS + (part + 1) * UNITS_PER_PART)
                    settle(sp)
                    load_ids(c, part)
                sp.wait_ge(transposed, (c - 1) * N_GATHERS + ROWS_FREE)
                settle(sp)
                load_index(c, p)

            def load_dense(c):
                sp.wait_ge(l1_full, (c + 1) * LAYER_BANKS)
                settle(sp)
                sp.dma_start(z[PAIR_ROWS:K_ROWS[0], 0, :],
                             dense_t[0:DENSE_ROWS[0], bass.ds(c * CHUNK, CHUNK)]).then_inc(z_ready, 16)
                sp.dma_start(z[PAIR_ROWS:K_ROWS[1], 1, :],
                             dense_t[DENSE_ROWS[0]:DENSE, bass.ds(c * CHUNK, CHUNK)]).then_inc(z_ready, 16)

            def store_grams(c):
                sp.wait_ge(gram_out_act, (c + 1) * N_GRAMS + GRAM_FREE)
                sp.wait_ge(gram_out_dve, (c + 1) * N_GRAMS + GRAM_FREE)
                settle(sp)
                sp.wait_ge(z_ready, c * Z_READS + DMA_FREE)
                settle(sp)
                for s in range(GROUP):
                    sp.dma_start(x_dram[:, :, s, :], gram[QUAD * s:QUAD * s + FEATURES, :, :]
                                 ).then_inc(x_written, 16)

            def load_pairs(c):
                sp.wait_ge(x_written, (c + 1) * X_WRITES + DMA_FREE)
                settle(sp)
                diagonal = (FEATURES + 1) * CHUNK
                for k in range(K_TILES):
                    src = bass.AP(x_dram.tensor, sum(N_TILES[:k]) * diagonal + CHUNK,
                                  [[diagonal, N_TILES[k]], [CHUNK, DIST], [1, CHUNK]])
                    sp.dma_start(z[0:N_TILES[k] * DIST, k, :], src).then_inc(z_ready, 16)
                src = bass.AP(x_dram.tensor, (DIST + 1) * CHUNK, [[diagonal, DIST], [1, CHUNK]])
                sp.dma_start(z[N_TILES[2] * DIST:PAIR_ROWS, 2, :], src).then_inc(z_ready, 16)

            def step(c, p):
                prefetch(c + 2, p)
                store_grams(c)
                load_dense(c)
                load_pairs(c)

            sp.wait_ge(z_cleared, 1)
            with sp.Fori(0, N_CHUNKS // 2 - 1) as i:
                step(i * 2, 0)
                step(i * 2 + 1, 1)
            store_grams(N_CHUNKS - 2)
            load_dense(N_CHUNKS - 2)
            load_pairs(N_CHUNKS - 2)
            last = N_CHUNKS - 1
            sp.wait_ge(z_ready, last * Z_READS + DMA_FREE)
            for h in range(HALVES):
                sp.wait_ge(gram_out_act, last * N_GRAMS + (h + 1) * N_GRAMS // HALVES + GRAM_FREE)
                sp.wait_ge(gram_out_dve, last * N_GRAMS + (h + 1) * N_GRAMS // HALVES + GRAM_FREE)
                t_half = slice(h * HALF_LANE, (h + 1) * HALF_LANE)
                for s in range(GROUP):
                    sp.dma_start(x_dram[:, :, s, t_half], gram[QUAD * s:QUAD * s + FEATURES, :, t_half]
                                 ).then_inc(x_written, 16)
            load_dense(last)
            sp.wait_ge(x_written, N_CHUNKS * X_WRITES + (HALVES - 1) * X_WRITES + DMA_FREE)
            load_pairs(last)
            sp.wait_ge(y_stored, 16 * N_CHUNKS + DMA_FREE)

        @block.gpsimd
        def _(pool):
            def gathers(c, p, use):
                pool.wait_ge(index_ready[p], (use + 1) * 16)
                settle(pool)
                for k in range(N_GATHERS):
                    h, g = divmod(k, len(SLOTS))
                    pool.wait_ge(transposed, c * N_GATHERS + k + 1)
                    settle(pool)
                    for j, n in enumerate(SLOTS[g]):
                        f = ORDER[n]
                        pool.indirect_dma_start(
                            rows[g][:, j * DIM:(j + 1) * DIM], None, tables[f],
                            bass.IndirectOffsetOnAxis(index[p][:, h, f:f + 1], 0)).then_inc(rows_in[g], 16)

            nc.gpsimd.iota(row_number_int[:, :], [[1, PART_ROWS]], base=0, channel_multiplier=PART_ROWS
                           ).then_inc(consts_ready, 1)
            nc.gpsimd.memset(identity[:, :], 0.0).then_inc(ident_zero, 1)
            pool.wait_ge(ident_zero, 1)
            nc.gpsimd.affine_select(out=identity[:, :], in_=identity[:, :], compare_op=ALU.not_equal, fill=1.0,
                                    base=0, pattern=[[-1, P]], channel_multiplier=1).then_inc(consts_ready, 1)
            with pool.Fori(0, N_CHUNKS // 2) as i:
                gathers(i * 2, 0, i)
                gathers(i * 2 + 1, 1, i)

        @block.tensor
        def _(pe):
            pe.sem_inc(transposed, ROWS_FREE)
            pe.sem_inc(unit_free, UNIT_RING)
            pe.sem_inc(l1_full, LAYER_BANKS)

            def gather(c, k):
                g = k % len(SLOTS)
                pe.wait_ge(rows_in[g], (c * HALVES + k // len(SLOTS) + 1) * 16 * len(SLOTS[g]))
                pe.wait_ge(gather_out, c * N_GATHERS + k + 1)
                for j in range(len(SLOTS[g])):
                    last = nc.tensor.transpose(gather_ps[k % GATHER_BANKS][:, j * P:(j + 1) * P],
                                               rows[g][:, j * DIM:(j + 1) * DIM], identity[:, :])
                last.then_inc(transposed, 1)

            def lookup_unit(c, u):
                k, part = divmod(u, UNITS_PER_TABLE)
                if part == 0:
                    pe.wait_ge(lookup_out, c * N_LOOKUP + k + 1)
                pe.wait_ge(unit_ready, c * N_UNITS + u + 1)
                for r in range(UNIT_ROWS):
                    row = part * UNIT_ROWS + r
                    for table in (table_hi, table_lo):
                        last = nc.tensor.matmul(lookup_ps[k % LOOKUP_BANKS], table[:, k, row, :],
                                                one_hot[u % UNIT_RING][:, r, :],
                                                start=(row == 0 and table is table_hi),
                                                stop=(row == PART_ROWS - 1 and table is table_lo))
                last.then_inc(unit_free, 1)

            def gram_bank(c, p, b):
                if b % (N_GRAMS // HALVES) == 0:
                    h = b // (N_GRAMS // HALVES)
                    pe.wait_ge(gather_out, (c * HALVES + h + 1) * len(SLOTS) + GATHER_FREE)
                    pe.wait_ge(lookup_out, (c + 1) * N_LOOKUP + LOOKUP_FREE)
                pe.wait_ge(gram_out_act, c * N_GRAMS + b + 1)
                pe.wait_ge(gram_out_dve, c * N_GRAMS + b + 1)
                for t in range(T_PER_BANK):
                    group = emb[p][:, b * T_PER_BANK + t, :, :]
                    last = nc.tensor.matmul(gram_ps[b % 2][0:USED_COLS, t * COLS:(t + 1) * COLS],
                                            group.rearrange("d s f -> d (s f)")[:, 0:USED_COLS],
                                            group[:, :, 0:FEATURES],
                                            start=True, stop=True)
                last.then_inc(gram_full, 1)

            def layer1(c):
                pe.wait_ge(z_split, c + 1)
                pe.wait_ge(y_ready, c + 1)
                for bank in range(LAYER_BANKS):
                    for j in range(TILES_PER_BANK):
                        o = bank * TILES_PER_BANK + j
                        halves = ((w1_hi, z_hi), (w1_hi, z_lo), (w1_lo, z_hi))
                        products = [(k, w_half, z_half) for k in range(K_TILES) for w_half, z_half in halves]
                        for n, (k, w_half, z_half) in enumerate(products):
                            last = nc.tensor.matmul(layer_ps[bank][:, j * CHUNK:(j + 1) * CHUNK],
                                                    w_half[0:K_ROWS[k], k, o * P:(o + 1) * P],
                                                    z_half[0:K_ROWS[k], k, :],
                                                    start=(n == 0), stop=(n == len(products) - 1))
                    last.then_inc(l1_full, 1)

            def layer2(c):
                for o in range(o2_tiles):
                    for k in range(o1_tiles):
                        if o == 0 and k % TILES_PER_BANK == 0:
                            pe.wait_ge(h1_ready, c * LAYER_BANKS + k // TILES_PER_BANK + 1)
                        last = nc.tensor.matmul(layer_ps[o][:, 0:CHUNK], w2_sb[:, k, o * P:(o + 1) * P], h1[:, k, :],
                                                start=(k == 0), stop=(k == o1_tiles - 1))
                    last.then_inc(l2_full, 1)

            def layer3(c):
                for k in range(o2_tiles):
                    pe.wait_ge(h2_ready, c * o2_tiles + k + 1)
                    last = nc.tensor.matmul(layer_ps[0][0:1, 0:CHUNK], w3_sb[:, k:k + 1], h2[:, k, :],
                                            start=(k == 0), stop=(k == o2_tiles - 1))
                last.then_inc(l3_full, 1)

            def run(c0, p0, order):
                for what, c, k in order:
                    if what == "gram":
                        gram_bank(c0 + c, (p0 + c) % 2, k)
                    elif what == "gather":
                        gather(c0 + c, k)
                    elif what == "unit":
                        lookup_unit(c0 + c, k)
                    elif what == "layer1":
                        layer1(c0 + c)
                    elif what == "layer2":
                        layer2(c0 + c)
                    elif what == "layer3":
                        layer3(c0 + c)

            pe.wait_ge(consts_ready, 2)
            for what, c, k in first_order():
                if what == "gather":
                    gather(c, k)
                else:
                    if c == 0 and k % UNITS_PER_TABLE == 0:
                        pe.wait_ge(table_hi_ready, k // UNITS_PER_TABLE + 1)
                        pe.wait_ge(table_lo_ready, k // UNITS_PER_TABLE + 1)
                    lookup_unit(c, k)
            pe.wait_ge(pad_ready, 2)
            pe.wait_ge(weights_in, WEIGHT_LOADS)
            pe.wait_ge(w1_split, 1)
            with pe.Fori(0, N_CHUNKS // 2 - 1) as i:
                run(i * 2, 0, step_order(0))
                run(i * 2, 0, step_order(1))
            run(0, 0, last_order())

        @block.scalar
        def _(act):
            act.sem_inc(gather_out, GATHER_FREE)
            act.sem_inc(lookup_out, LOOKUP_FREE)
            act.sem_inc(gram_out_act, GRAM_FREE)
            act.sem_inc(y_ready, 1)
            act.sem_inc(y_stored, DMA_FREE)

            def copy_gather(c, p, k):
                h, g = divmod(k, len(SLOTS))
                n0, n = SLOTS[g][0], len(SLOTS[g])
                act.wait_ge(transposed, c * N_GATHERS + k + 1 + ROWS_FREE)
                dst = emb[p][:, h * HALF_LANE:(h + 1) * HALF_LANE, :, n0:n0 + n].rearrange("d t s f -> d f s t")
                src = gather_ps[k % GATHER_BANKS][:, 0:n * P].rearrange("d (f s t) -> d f s t", f=n, s=GROUP)
                nc.scalar.activation(dst, src, ACT.Copy).then_inc(gather_out, 1)

            def copy_lookup(c, p, k):
                act.wait_ge(unit_free, c * N_UNITS + (k + 1) * UNITS_PER_TABLE + UNIT_RING)
                src = lookup_ps[k % LOOKUP_BANKS].rearrange("d (s t) -> d s t", s=GROUP)
                dst = emb[p][:, :, :, len(GATHER) + k].rearrange("d t s -> d s t")
                nc.scalar.activation(dst, src, ACT.Copy).then_inc(lookup_out, 1)

            def relu1(c):
                for bank in range(LAYER_BANKS):
                    act.wait_ge(l1_full, (c + 1) * LAYER_BANKS + bank + 1)
                    for j in range(TILES_PER_BANK):
                        o = bank * TILES_PER_BANK + j
                        last = nc.scalar.activation(h1[:, o, :], layer_ps[bank][:, j * CHUNK:(j + 1) * CHUNK],
                                                    ACT.Relu, bias=b1_sb[:, o:o + 1])
                    last.then_inc(h1_ready, 1)

            def relu2(c):
                for o in range(o2_tiles):
                    act.wait_ge(l2_full, c * o2_tiles + o + 1)
                    nc.scalar.activation(h2[:, o, :], layer_ps[o][:, 0:CHUNK], ACT.Relu, bias=b2_sb[:, o:o + 1]
                                         ).then_inc(h2_ready, 1)

            def copy_y(c):
                act.wait_ge(l3_full, c + 1)
                act.wait_ge(y_stored, c * 16 + DMA_FREE)
                nc.scalar.activation(y_sb[:, :], layer_ps[0][0:1, 0:CHUNK], ACT.Copy).then_inc(y_ready, 1)
                act.wait_ge(y_ready, c + 2)
                settle(act)
                act.dma_start(y_out[bass.ds(c * CHUNK, CHUNK), :].rearrange("b o -> o b"),
                              y_sb[:, :]).then_inc(y_stored, 16)

            def run(c0, p0, order):
                for what, c, k in order:
                    if what == "gram":
                        if k == 0:
                            act.wait_ge(x_written, (c0 + c) * X_WRITES + DMA_FREE)
                        act.wait_ge(gram_full, (c0 + c) * N_GRAMS + k + 1)
                        copy_grams(nc.scalar.copy, k, (0, 1), gram_out_act)
                    elif what == "gather":
                        copy_gather(c0 + c, (p0 + c) % 2, k)
                    elif what == "unit":
                        if k % UNITS_PER_TABLE == UNITS_PER_TABLE - 1:
                            copy_lookup(c0 + c, (p0 + c) % 2, k // UNITS_PER_TABLE)
                    elif what == "layer1":
                        relu1(c0 + c)
                    elif what == "layer2":
                        relu2(c0 + c)
                    elif what == "layer3":
                        copy_y(c0 + c)

            def table_high(k):
                act.wait_ge(stage_in[k % STAGES], (k // STAGES + 1) * 16)
                nc.scalar.activation(table_hi[:, k, :, :].rearrange("p r d -> p (r d)"), stage(k % STAGES), ACT.Copy
                                     ).then_inc(table_hi_ready, 1)

            act.wait_ge(w1_in, W1_LOADS)
            for k in range(K_TILES):
                last = nc.scalar.activation(w1_hi[0:K_ROWS[k], k, :], w1_sb[0:K_ROWS[k], k, :], ACT.Copy)
            last.then_inc(w1_hi_ready, 1)
            for n in range(TABLES_AHEAD):
                table_high(n)
            for what, c, k in first_order():
                table, part = divmod(k, UNITS_PER_TABLE)
                if what == "gather":
                    copy_gather(c, c, k)
                elif part == UNITS_PER_TABLE - 1:
                    if c == 0 and table + TABLES_AHEAD < N_LOOKUP:
                        table_high(table + TABLES_AHEAD)
                    if c == 1:
                        act.wait_ge(table_lo_ready, N_LOOKUP)
                    copy_lookup(c, c, table)
            act.wait_ge(weights_in, WEIGHT_LOADS)
            act.wait_ge(w1_split, 1)
            with act.Fori(0, N_CHUNKS // 2 - 1) as i:
                run(i * 2, 0, step_order(0))
                run(i * 2, 0, step_order(1))
            run(0, 0, last_order())

        @block.vector
        def _(dve):
            dve.sem_inc(gram_out_dve, GRAM_FREE)

            def make_unit(c, u):
                k, part = divmod(u, UNITS_PER_TABLE)
                if u % UNITS_PER_PART == 0:
                    dve.wait_ge(ids_ready[u // UNITS_PER_PART], (c + 1) * 16)
                dve.wait_ge(unit_free, c * N_UNITS + u + 1)
                table_ids = ids_all[u // UNITS_PER_PART][0:LOOKUP_PARTS, k % TABLES_PER_PART, :]
                for r in range(UNIT_ROWS):
                    row = part * UNIT_ROWS + r
                    last = nc.vector.tensor_scalar(one_hot[u % UNIT_RING][:, r, :], table_ids,
                                                   row_number[0:LOOKUP_PARTS, row:row + 1], None, ALU.is_equal)
                last.then_inc(unit_ready, 1)

            def table_low(k):
                dve.wait_ge(table_hi_ready, k + 1)
                nc.vector.tensor_tensor(table_lo[:, k, :, :].rearrange("p r d -> p (r d)"), stage(k % STAGES),
                                        table_hi[:, k, :, :].rearrange("p r d -> p (r d)").bitcast(fp32),
                                        ALU.subtract).then_inc(table_lo_ready, 1)

            def split_z(c):
                dve.wait_ge(z_ready, (c + 1) * Z_READS + DMA_FREE)
                nc.vector.tensor_copy(z_hi[:, :, :], z[:, :, :]).then_inc(z_hi_ready, 1)
                dve.wait_ge(z_hi_ready, c + 1)
                nc.vector.tensor_tensor(z_lo[:, :, :], z[:, :, :], z_hi[:, :, :].bitcast(fp32), ALU.subtract
                                        ).then_inc(z_split, 1)

            def run(c0, order, end=None):
                for what, c, k in order:
                    if what == "gram":
                        if k == 0:
                            dve.wait_ge(x_written, (c0 + c) * X_WRITES + DMA_FREE)
                        dve.wait_ge(gram_full, (c0 + c) * N_GRAMS + k + 1)
                        copy_grams(nc.vector.tensor_copy, k, (2, 3), gram_out_dve)
                    elif what == "unit":
                        ahead, u = divmod(k + UNIT_RING, N_UNITS)
                        if end is None or (c + ahead) * N_UNITS + u < end:
                            make_unit(c0 + c + ahead, u)
                    elif what == "split":
                        split_z(c0 + c)

            nc.vector.memset(emb[0][:, :, :, FEATURES:], 0.0).then_inc(pad_ready, 1)
            nc.vector.memset(z[:, :, :], 0.0).then_inc(z_cleared, 1)
            dve.wait_ge(consts_ready, 1)
            nc.vector.tensor_copy(row_number[:, :], row_number_int[:, :]).then_inc(row_number_ready, 1)
            dve.wait_ge(row_number_ready, 1)
            dve.wait_ge(w1_hi_ready, 1)
            for k in range(K_TILES):
                last = nc.vector.tensor_tensor(w1_lo[0:K_ROWS[k], k, :], w1_sb[0:K_ROWS[k], k, :],
                                               w1_hi[0:K_ROWS[k], k, :].bitcast(fp32), ALU.subtract)
            last.then_inc(w1_split, 1)
            for k in range(N_LOOKUP):
                table_low(k)
                for u in range(k * UNITS_PER_TABLE, (k + 1) * UNITS_PER_TABLE):
                    make_unit(0, u)
            dve.wait_ge(table_lo_ready, N_LOOKUP)
            nc.vector.memset(emb[1][:, :, :, FEATURES:], 0.0).then_inc(pad_ready, 1)
            for u in range(EARLY_UNITS + UNIT_RING):
                make_unit(1, u)
            dve.wait_ge(w1_split, 1)
            with dve.Fori(0, N_CHUNKS // 2 - 1) as i:
                run(i * 2, step_order(0))
                run(i * 2, step_order(1))
            run(0, last_order(), N_CHUNKS * N_UNITS)


def layer1_row_order():
    order, dense = [], FEATURES * (FEATURES - 1) // 2
    for k in range(K_TILES):
        n0 = sum(N_TILES[:k])
        elements = [n * (FEATURES + 1) + d for n in range(n0, n0 + N_TILES[k]) for d in range(1, DIST + 1)]
        if k == 2:
            elements += [n * (FEATURES + 1) + DIST + 1 for n in range(DIST)]
        for m, n in (divmod(e, FEATURES) for e in elements):
            hi, lo = max(ORDER[n], ORDER[m]), min(ORDER[n], ORDER[m])
            order.append(hi * (hi - 1) // 2 + lo)
        order += list(range(dense, dense + DENSE_ROWS[k]))
        dense += DENSE_ROWS[k]
    return order


def kernel(**inputs):
    import numpy as np
    import concourse.bacc as bacc
    from concourse.bass_utils import run_bass_kernel_spmd

    def columns(v):
        return np.ascontiguousarray(np.asarray(v).reshape(-1, P).T)

    ids = np.asarray(inputs["ids"])
    nc = bacc.Bacc("TRN2", target_bir_lowering=False, num_devices=1)
    arrays = {
        "dense_t": np.ascontiguousarray(np.asarray(inputs["dense_ctx"]).T),
        "ids": np.ascontiguousarray(ids.reshape(N_CHUNKS, GROUP, HALVES, HALF_LANE, FEATURES).transpose(0, 2, 1, 3, 4)
                                    .reshape(BATCH, FEATURES)),
        "lookup_ids": np.ascontiguousarray(ids.T[LOOKUP]),
        "w1": np.ascontiguousarray(np.asarray(inputs["W_top1"])[layer1_row_order()]),
        "b1": columns(inputs["b_top1"]),
        "w2": np.asarray(inputs["W_top2"]),
        "b2": columns(inputs["b_top2"]),
        "w3": columns(inputs["W_top3"]),
    }
    for f in range(FEATURES):
        arrays[f"tbl_{f}"] = np.asarray(inputs[f"tbl_{f}"])
    aps = {k: nc.dram_tensor(k, v.shape, mybir.dt.from_np(v.dtype), kind="ExternalInput").ap()
           for k, v in arrays.items()}
    y = nc.dram_tensor("y", (BATCH, 1), mybir.dt.float32, kind="ExternalOutput").ap()
    dlrm_tower(nc, aps["dense_t"], aps["ids"], aps["lookup_ids"], [aps[f"tbl_{f}"] for f in range(FEATURES)],
               aps["w1"], aps["b1"], aps["w2"], aps["b2"], aps["w3"], y)
    result = run_bass_kernel_spmd(nc, [arrays], core_ids=[0])
    return result.results[0]["y"]
```
